# Optimizing a Trainium2 kernel written in Bass

```python
import numpy as np
import jax
import jax.numpy as jnp

def _softmax(x, axis=-1):
    return jax.nn.softmax(x, axis=axis)

def _gelu(x):
    return jax.nn.gelu(x, approximate=True)

def _silu(x):
    return jax.nn.silu(x)

def _sigmoid(x):
    return jax.nn.sigmoid(x)

def _layernorm(x, axis=-1, eps=1e-05):
    m = jnp.mean(x, axis=axis, keepdims=True)
    v = jnp.var(x, axis=axis, keepdims=True)
    return (x - m) / jnp.sqrt(v + eps)

def _scatter_add(tgt, idx, src, axis=0):
    return tgt.at[idx].add(src)

def _segment_sum(src, seg, n):
    return jax.ops.segment_sum(src, seg, n)
kernel_name = 'mk_audio_tower_d1_tok_audfeat512_r4_f71301'

def setup_inputs(seed: int=0):
    np.random.seed(seed)
    _w = jnp.asarray

    def _rec_inputs():
        import jax
        import jax.numpy as jnp
        _rk = jax.random.key(seed)
        x = -0.0003702 + 0.999946 * jax.random.normal(jax.random.fold_in(_rk, 1), (64, 750, 64), jnp.float32)
        return x
    x = _rec_inputs()

    def _L0_tok_setup():
        import jax, jax.numpy as jnp
        import numpy as np
        CONTEXT_LEN = 3
        SUBSAMPLING = 3
        key = jax.random.key(seed)
        k1, k2, k3 = jax.random.split(key, 3)
        B, T, D = (32, 500, 64)
        OUT = 128
        x = jax.random.normal(k1, (B, T, D), dtype=jnp.float32)
        weight = jax.random.normal(k2, (OUT, D * CONTEXT_LEN), dtype=jnp.float32)
        weight = weight * (1.0 / np.sqrt(D * CONTEXT_LEN * OUT).astype(np.float32))
        bias = jax.random.normal(k3, (1, OUT), dtype=jnp.float32)
        return {'x': x, 'weight': weight, 'bias': bias}
    _L0_tok_all = _L0_tok_setup()
    _L0_tok_in = {k: v for k, v in _L0_tok_all.items() if k in ('weight', 'bias')}
    del _L0_tok_all

    def _L0_attn_setup():
        import jax, jax.numpy as jnp
        import numpy as np
        D_MODEL = 128
        D_STATE = 16
        D_CONV = 4
        D_INNER = 2 * D_MODEL
        DT_RANK = (D_MODEL + 15) // 16
        LN_EPS = 1e-05

        def _mamba_params(key):
            ks = jax.random.split(key, 6)

            def nrm(k, shape, s=0.02):
                return jax.random.normal(k, shape, jnp.float32) * s
            return dict(in_proj=nrm(ks[0], (2 * D_INNER, D_MODEL)), conv_w=nrm(ks[1], (D_INNER, D_CONV), 0.2), conv_b=jnp.zeros((D_INNER,), jnp.float32), x_proj=nrm(ks[2], (DT_RANK + 2 * D_STATE, D_INNER)), dt_w=nrm(ks[3], (D_INNER, DT_RANK), 0.1), dt_b=jax.random.uniform(ks[4], (D_INNER,), jnp.float32, -4.0, -2.0), A_log=jnp.log(jnp.tile(jnp.arange(1, D_STATE + 1, dtype=jnp.float32), (D_INNER, 1))), Dv=jnp.ones((D_INNER,), jnp.float32), out_proj=nrm(ks[5], (D_MODEL, D_INNER)))

        def _mamba(x, in_proj, conv_w, conv_b, x_proj, dt_w, dt_b, A_log, Dv, out_proj):
            B, L, _ = x.shape
            xz = jnp.einsum('bld,ed->ble', x, in_proj)
            xi, z = jnp.split(xz, 2, axis=-1)
            xc = jnp.transpose(xi, (0, 2, 1))
            xc = jax.lax.conv_general_dilated(xc, conv_w[:, None, :], window_strides=(1,), padding=[(D_CONV - 1, 0)], feature_group_count=D_INNER)
            xc = jax.nn.silu(jnp.transpose(xc, (0, 2, 1)) + conv_b)
            dbl = jnp.einsum('ble,fe->blf', xc, x_proj)
            dt, Bm, Cm = jnp.split(dbl, [DT_RANK, DT_RANK + D_STATE], axis=-1)
            delta = jax.nn.softplus(jnp.einsum('blr,er->ble', dt, dt_w) + dt_b)
            A = -jnp.exp(A_log)

            def step(h, inp):
                xt, dt_, bt, ct = inp
                dA = jnp.exp(dt_[..., None] * A)
                h = dA * h + dt_[..., None] * bt[:, None, :] * xt[..., None]
                y = jnp.einsum('bdn,bn->bd', h, ct)
                return (h, y)
            xs = (jnp.swapaxes(xc, 0, 1), jnp.swapaxes(delta, 0, 1), jnp.swapaxes(Bm, 0, 1), jnp.swapaxes(Cm, 0, 1))
            h0 = jnp.zeros((B, D_INNER, D_STATE), x.dtype)
            _, ys = jax.lax.scan(step, h0, xs)
            y = jnp.swapaxes(ys, 0, 1) + xc * Dv
            y = y * jax.nn.silu(z)
            return jnp.einsum('ble,de->bld', y, out_proj)

        def _layernorm(x, g, b):
            mu = jnp.mean(x, axis=-1, keepdims=True)
            var = jnp.mean(jnp.square(x - mu), axis=-1, keepdims=True)
            return (x - mu) * jax.lax.rsqrt(var + LN_EPS) * g + b
        key = jax.random.key(seed)
        kx, kf, kb, kg = jax.random.split(key, 4)
        x = jax.random.normal(kx, (8, 256, D_MODEL), jnp.float32)
        pf = _mamba_params(kf)
        pb = _mamba_params(kb)
        inp = {'x': x}
        for pre, p in (('f_', pf), ('b_', pb)):
            for name, v in p.items():
                inp[pre + name] = v
        inp['ln_g'] = jnp.ones((D_MODEL,), jnp.float32)
        inp['ln_b'] = jnp.zeros((D_MODEL,), jnp.float32)
        return inp
    _L0_attn_all = _L0_attn_setup()
    _L0_attn_in = {k: v for k, v in _L0_attn_all.items() if k in ('f_in_proj', 'f_conv_w', 'f_conv_b', 'f_x_proj', 'f_dt_w', 'f_dt_b', 'f_A_log', 'f_Dv', 'f_out_proj', 'b_in_proj', 'b_conv_w', 'b_conv_b', 'b_x_proj', 'b_dt_w', 'b_dt_b', 'b_A_log', 'b_Dv', 'b_out_proj', 'ln_g', 'ln_b')}
    del _L0_attn_all

    def _L0_ffn_setup():
        import jax, jax.numpy as jnp
        import numpy as np
        MARK_AX = 0
        OP_MUL = 1
        OPCODE_BASE = 2
        ALU_LO, ALU_HI = (64, 80)
        AX_CARRY_LO, AX_CARRY_HI = (96, 112)
        OUTPUT_LO, OUTPUT_HI = (128, 144)
        NIB_A, NIB_B, RESULT, OP_START = (0, 1, 2, 3)
        GE_DIM = 160
        N_POS = 8
        N_LAYERS = 7
        OPCODE = 27

        def _decode_nibble(x16):
            return jnp.argmax(x16 > 0.5, axis=-1).astype(x16.dtype)
        key = jax.random.key(seed)
        k1, k2, k3 = jax.random.split(key, 3)
        x_bd = jax.random.uniform(k1, (4, 2048, 128), dtype=jnp.float32)
        W = jax.random.normal(k2, (N_LAYERS, GE_DIM, GE_DIM), dtype=jnp.float32) * 0.05
        b = jax.random.normal(k3, (N_LAYERS, GE_DIM), dtype=jnp.float32) * 0.01
        return {'x_bd': x_bd, 'W': W, 'b': b}
    _L0_ffn_all = _L0_ffn_setup()
    _L0_ffn_in = {k: v for k, v in _L0_ffn_all.items() if k in ('W', 'b')}
    del _L0_ffn_all
    return {'x': x, 'L0_tok_weight': _L0_tok_in['weight'], 'L0_tok_bias': _L0_tok_in['bias'], 'L0_attn_f_in_proj': _L0_attn_in['f_in_proj'], 'L0_attn_f_conv_w': _L0_attn_in['f_conv_w'], 'L0_attn_f_conv_b': _L0_attn_in['f_conv_b'], 'L0_attn_f_x_proj': _L0_attn_in['f_x_proj'], 'L0_attn_f_dt_w': _L0_attn_in['f_dt_w'], 'L0_attn_f_dt_b': _L0_attn_in['f_dt_b'], 'L0_attn_f_A_log': _L0_attn_in['f_A_log'], 'L0_attn_f_Dv': _L0_attn_in['f_Dv'], 'L0_attn_f_out_proj': _L0_attn_in['f_out_proj'], 'L0_attn_b_in_proj': _L0_attn_in['b_in_proj'], 'L0_attn_b_conv_w': _L0_attn_in['b_conv_w'], 'L0_attn_b_conv_b': _L0_attn_in['b_conv_b'], 'L0_attn_b_x_proj': _L0_attn_in['b_x_proj'], 'L0_attn_b_dt_w': _L0_attn_in['b_dt_w'], 'L0_attn_b_dt_b': _L0_attn_in['b_dt_b'], 'L0_attn_b_A_log': _L0_attn_in['b_A_log'], 'L0_attn_b_Dv': _L0_attn_in['b_Dv'], 'L0_attn_b_out_proj': _L0_attn_in['b_out_proj'], 'L0_attn_ln_g': _L0_attn_in['ln_g'], 'L0_attn_ln_b': _L0_attn_in['ln_b'], 'L0_ffn_W': _L0_ffn_in['W'], 'L0_ffn_b': _L0_ffn_in['b']}

def reference(x, L0_tok_weight, L0_tok_bias, L0_attn_f_in_proj, L0_attn_f_conv_w, L0_attn_f_conv_b, L0_attn_f_x_proj, L0_attn_f_dt_w, L0_attn_f_dt_b, L0_attn_f_A_log, L0_attn_f_Dv, L0_attn_f_out_proj, L0_attn_b_in_proj, L0_attn_b_conv_w, L0_attn_b_conv_b, L0_attn_b_x_proj, L0_attn_b_dt_w, L0_attn_b_dt_b, L0_attn_b_A_log, L0_attn_b_Dv, L0_attn_b_out_proj, L0_attn_ln_g, L0_attn_ln_b, L0_ffn_W, L0_ffn_b):
    import jax
    import jax.numpy as jnp

    def _L0_tok_ref(x, weight, bias):
        import jax, jax.numpy as jnp
        import numpy as np
        CONTEXT_LEN = 3
        SUBSAMPLING = 3
        B, T, D = x.shape
        l = CONTEXT_LEN
        N = T - l + 1
        spliced = jnp.concatenate([x[:, i:i + N, :] for i in range(l)], axis=-1)
        spliced = spliced[:, ::SUBSAMPLING, :]
        return jnp.einsum('bnk,ok->bno', spliced, weight) + bias[0]

    def _L0_attn_ref(x, f_in_proj, f_conv_w, f_conv_b, f_x_proj, f_dt_w, f_dt_b, f_A_log, f_Dv, f_out_proj, b_in_proj, b_conv_w, b_conv_b, b_x_proj, b_dt_w, b_dt_b, b_A_log, b_Dv, b_out_proj, ln_g, ln_b):
        import jax, jax.numpy as jnp
        import numpy as np
        D_MODEL = 128
        D_STATE = 16
        D_CONV = 4
        D_INNER = 2 * D_MODEL
        DT_RANK = (D_MODEL + 15) // 16
        LN_EPS = 1e-05

        def _mamba_params(key):
            ks = jax.random.split(key, 6)

            def nrm(k, shape, s=0.02):
                return jax.random.normal(k, shape, jnp.float32) * s
            return dict(in_proj=nrm(ks[0], (2 * D_INNER, D_MODEL)), conv_w=nrm(ks[1], (D_INNER, D_CONV), 0.2), conv_b=jnp.zeros((D_INNER,), jnp.float32), x_proj=nrm(ks[2], (DT_RANK + 2 * D_STATE, D_INNER)), dt_w=nrm(ks[3], (D_INNER, DT_RANK), 0.1), dt_b=jax.random.uniform(ks[4], (D_INNER,), jnp.float32, -4.0, -2.0), A_log=jnp.log(jnp.tile(jnp.arange(1, D_STATE + 1, dtype=jnp.float32), (D_INNER, 1))), Dv=jnp.ones((D_INNER,), jnp.float32), out_proj=nrm(ks[5], (D_MODEL, D_INNER)))

        def _mamba(x, in_proj, conv_w, conv_b, x_proj, dt_w, dt_b, A_log, Dv, out_proj):
            B, L, _ = x.shape
            xz = jnp.einsum('bld,ed->ble', x, in_proj)
            xi, z = jnp.split(xz, 2, axis=-1)
            xc = jnp.transpose(xi, (0, 2, 1))
            xc = jax.lax.conv_general_dilated(xc, conv_w[:, None, :], window_strides=(1,), padding=[(D_CONV - 1, 0)], feature_group_count=D_INNER)
            xc = jax.nn.silu(jnp.transpose(xc, (0, 2, 1)) + conv_b)
            dbl = jnp.einsum('ble,fe->blf', xc, x_proj)
            dt, Bm, Cm = jnp.split(dbl, [DT_RANK, DT_RANK + D_STATE], axis=-1)
            delta = jax.nn.softplus(jnp.einsum('blr,er->ble', dt, dt_w) + dt_b)
            A = -jnp.exp(A_log)

            def step(h, inp):
                xt, dt_, bt, ct = inp
                dA = jnp.exp(dt_[..., None] * A)
                h = dA * h + dt_[..., None] * bt[:, None, :] * xt[..., None]
                y = jnp.einsum('bdn,bn->bd', h, ct)
                return (h, y)
            xs = (jnp.swapaxes(xc, 0, 1), jnp.swapaxes(delta, 0, 1), jnp.swapaxes(Bm, 0, 1), jnp.swapaxes(Cm, 0, 1))
            h0 = jnp.zeros((B, D_INNER, D_STATE), x.dtype)
            _, ys = jax.lax.scan(step, h0, xs)
            y = jnp.swapaxes(ys, 0, 1) + xc * Dv
            y = y * jax.nn.silu(z)
            return jnp.einsum('ble,de->bld', y, out_proj)

        def _layernorm(x, g, b):
            mu = jnp.mean(x, axis=-1, keepdims=True)
            var = jnp.mean(jnp.square(x - mu), axis=-1, keepdims=True)
            return (x - mu) * jax.lax.rsqrt(var + LN_EPS) * g + b
        f = _mamba(x, f_in_proj, f_conv_w, f_conv_b, f_x_proj, f_dt_w, f_dt_b, f_A_log, f_Dv, f_out_proj)
        x_rev = jnp.flip(x, axis=1)
        b = jnp.flip(_mamba(x_rev, b_in_proj, b_conv_w, b_conv_b, b_x_proj, b_dt_w, b_dt_b, b_A_log, b_Dv, b_out_proj), axis=1)
        out = (f + b) * 0.5
        return _layernorm(out + x, ln_g, ln_b)

    def _L0_ffn_ref(x_bd, W, b):
        import jax, jax.numpy as jnp
        import numpy as np
        MARK_AX = 0
        OP_MUL = 1
        OPCODE_BASE = 2
        ALU_LO, ALU_HI = (64, 80)
        AX_CARRY_LO, AX_CARRY_HI = (96, 112)
        OUTPUT_LO, OUTPUT_HI = (128, 144)
        NIB_A, NIB_B, RESULT, OP_START = (0, 1, 2, 3)
        GE_DIM = 160
        N_POS = 8
        N_LAYERS = 7
        OPCODE = 27

        def _decode_nibble(x16):
            return jnp.argmax(x16 > 0.5, axis=-1).astype(x16.dtype)
        B, S, D = x_bd.shape
        mask = (x_bd[..., MARK_AX] >= 0.5) & (x_bd[..., OP_MUL] >= 0.5)
        a_lo = _decode_nibble(x_bd[..., ALU_LO:ALU_LO + 16])
        a_hi = _decode_nibble(x_bd[..., ALU_HI:ALU_HI + 16])
        b_lo = _decode_nibble(x_bd[..., AX_CARRY_LO:AX_CARRY_LO + 16])
        b_hi = _decode_nibble(x_bd[..., AX_CARRY_HI:AX_CARRY_HI + 16])
        op_val = x_bd[..., OPCODE_BASE + OPCODE]
        x_ge = jnp.zeros((B, S, N_POS, GE_DIM), dtype=x_bd.dtype)
        x_ge = x_ge.at[..., 0, NIB_A].set(a_lo)
        x_ge = x_ge.at[..., 1, NIB_A].set(a_hi)
        x_ge = x_ge.at[..., 0, NIB_B].set(b_lo)
        x_ge = x_ge.at[..., 1, NIB_B].set(b_hi)
        x_ge = x_ge.at[..., :, OP_START + OPCODE].set(op_val[..., None])
        h = x_ge
        for i in range(N_LAYERS):
            h = jnp.einsum('bspd,ed->bspe', h, W[i]) + b[i]
            if i < N_LAYERS - 1:
                h = jax.nn.relu(h)
        res_lo = jnp.clip(jnp.round(h[..., 0, RESULT]), 0, 15).astype(jnp.int32)
        res_hi = jnp.clip(jnp.round(h[..., 1, RESULT]), 0, 15).astype(jnp.int32)
        m = mask[..., None].astype(x_bd.dtype)
        add_lo = 2.0 * jax.nn.one_hot(res_lo, 16, dtype=x_bd.dtype) * m
        add_hi = 2.0 * jax.nn.one_hot(res_hi, 16, dtype=x_bd.dtype) * m
        out = x_bd.at[..., OUTPUT_LO:OUTPUT_LO + 16].add(add_lo)
        out = out.at[..., OUTPUT_HI:OUTPUT_HI + 16].add(add_hi)
        return out
    h = _L0_tok_ref(x, L0_tok_weight, L0_tok_bias)
    h = h + _L0_attn_ref(_layernorm(h, axis=-1), L0_attn_f_in_proj, L0_attn_f_conv_w, L0_attn_f_conv_b, L0_attn_f_x_proj, L0_attn_f_dt_w, L0_attn_f_dt_b, L0_attn_f_A_log, L0_attn_f_Dv, L0_attn_f_out_proj, L0_attn_b_in_proj, L0_attn_b_conv_w, L0_attn_b_conv_b, L0_attn_b_x_proj, L0_attn_b_dt_w, L0_attn_b_dt_b, L0_attn_b_A_log, L0_attn_b_Dv, L0_attn_b_out_proj, L0_attn_ln_g, L0_attn_ln_b)
    h = h + _L0_ffn_ref(_layernorm(h, axis=-1), L0_ffn_W, L0_ffn_b)
    return h

_drawn_inputs = setup_inputs


def setup_inputs(seed=0):
    import zlib

    import numpy as np

    out = dict(_drawn_inputs(seed))
    spreads = {'L0_attn_f_conv_b': (0.0, 0.8),
     'L0_attn_f_Dv': (1.0, 0.6),
     'L0_attn_b_conv_b': (0.0, 0.8),
     'L0_attn_b_Dv': (1.0, 0.6),
     'L0_attn_ln_g': (1.0, 0.2),
     'L0_attn_ln_b': (0.0, 0.1)}
    factors = {'L0_attn_f_in_proj': 8.0,
     'L0_attn_f_conv_w': 8.0,
     'L0_attn_f_x_proj': 8.0,
     'L0_attn_f_dt_w': 8.0,
     'L0_attn_f_dt_b': 8.0,
     'L0_attn_f_A_log': 8.0,
     'L0_attn_f_out_proj': 8.0,
     'L0_attn_b_in_proj': 8.0,
     'L0_attn_b_conv_w': 8.0,
     'L0_attn_b_x_proj': 8.0,
     'L0_attn_b_dt_w': 8.0,
     'L0_attn_b_dt_b': 8.0,
     'L0_attn_b_A_log': 8.0,
     'L0_attn_b_out_proj': 8.0}
    for name, (base, spread) in spreads.items():
        noise = np.random.default_rng([zlib.crc32(name.encode()), seed]).standard_normal(out[name].shape)
        drawn = base * np.exp(spread * noise) if base else spread * noise
        out[name] = jnp.asarray(drawn.astype(out[name].dtype))
    for name, factor in factors.items():
        out[name] = (out[name] * factor).astype(out[name].dtype)
    return out
```

```python
from contextlib import ExitStack

import concourse.bass as bass
from concourse import mybir

F32 = mybir.dt.float32
BF16 = mybir.dt.bfloat16
ALU = mybir.AluOpType
ACT = mybir.ActivationFunctionType

SEQS, T, DM = 64, 250, 128
K2 = 96
DI, NS, RANK = 256, 16, 8
TAPS = 4
SC = 2
TC = SC * T
NCH = SEQS // SC
TP, NT = 125, 4
PAD = TAPS - 1
TW = T + 2 * PAD
PAIRS = NS // 2
UNITS = 2 * PAIRS
UC = 2 * TC
RING = 4
XR = 3 * 2 * NS + RANK
DT0 = 3 * 2 * NS
BANK = 512
EPS = 1e-5

JOBS_FRONT = 7 + NS
JOBS_TOKENS = 2
JOBS_TAIL = 2
JOBS_CHUNK = 2 * JOBS_FRONT + JOBS_TOKENS + JOBS_TAIL
JOBS_AHEAD = JOBS_TOKENS + JOBS_FRONT


def jobs_before(i):
    if isinstance(i, int) and i == 0:
        return JOBS_AHEAD
    if isinstance(i, int) and i == NCH:
        return JOBS_CHUNK * i - JOBS_TAIL
    return JOBS_CHUNK * i + (JOBS_AHEAD - JOBS_TAIL)


def job(c, what, d=0, n=0):
    if what == "tail":
        start = jobs_before(c + 1)
        return start + ((1 if isinstance(c, int) and c == NCH - 1 else 6) + n)
    start = jobs_before(c) - JOBS_AHEAD * (1 - d)
    first = {"tokens": 1, "turn": 2}
    if what in first:
        return start + first[what]
    ahead_of = JOBS_TOKENS if d == 0 else 0
    tails = JOBS_TAIL if d == 1 and not (isinstance(c, int) and c == 0) else 0
    at = {"conv": 1, "gate": 3, "xproj": 5, "dt": 6 + tails, "c": 8 + tails}[what]
    return start + (ahead_of + at + n)


def bank_of(c, what, d=0, n=0):
    return (job(c if isinstance(c, int) else 2, what, d, n) - 1) % 2


def back(i, d, k, by):
    k -= by
    if k < 0:
        k, d = k + UNITS, d - 1
    if d < 0:
        d, i = d + 2, i - 1
    return None if isinstance(i, int) and i < 0 else (i, d, k)


def ahead(i, d, k, by):
    k += by
    if k >= UNITS:
        k, d = k - UNITS, d + 1
    if d > 1:
        d, i = d - 2, i + 1
    return None if isinstance(i, int) and i >= NCH else (i, d, k)


def nth(i, d, k):
    return 2 * UNITS * i + (UNITS * d + k)


def late(count):
    return not isinstance(count, int) or count > 0


C_SLOTS = {9: (0, 3), 10: (3, 6), 11: (6, 8), 12: (8, 10), 13: (10, 12), 14: (12, 14), 15: (14, 16)}


def audio_tower_kernel(nc, x_t, tok_w, tok_b, dirs, ln_g, ln_b, eye, eye3, out):
    with ExitStack() as ctx:
        def sb(name, shape, dt=F32):
            return ctx.enter_context(nc.sbuf_tensor(name, shape, dt))

        def sem(name):
            return ctx.enter_context(nc.semaphore(name))

        tokw = sb("tokw", [K2, 2, DM])
        tokb = sb("tokb", [TP, DM])
        lng = sb("lng", [TP, DM])
        lnb = sb("lnb", [TP, DM])
        ident = sb("ident", [128, 128])
        eyes = sb("eyes", [K2, 32])
        pick = sb("pick", [K2, 32, 128], BF16)
        inw = [sb(f"inw{d}", [128, 2 * DI]) for d in range(2)]
        convw = [sb(f"convw{d}", [128, TAPS, DI]) for d in range(2)]
        convb = sb("convb", [128, 2, 2])
        xpw = sb("xpw", [128, 2, 2, XR])
        dtw = sb("dtw", [XR, 2, DI])
        dtb = sb("dtb", [128, 2, 2])
        a_neg = sb("a_neg", [128, 2, 2, NS])
        dskip = sb("dskip", [128, 2, 2])
        outw = sb("outw", [128, 2, 2, DM])
        half = sb("half", [TP, NT])
        ones = sb("ones", [128, 2])
        xin = sb("xin", [K2, 2, TC])
        h0 = sb("h0", [TP, NT, DM])
        z = sb("z", [TP, NT, DM])
        zt = sb("zt", [128, SC, TW])
        h0b_kept = sb("h0b_kept", [TP, NT, DM])
        z_kept = sb("z_kept", [TP, NT, DM])
        stats = sb("stats", [TP, 3, NT, 6])
        meanvar = sb("meanvar", [TP, 3, NT, 2])
        vareps = sb("vareps", [TP, 3, NT])
        rstd = sb("rstd", [TP, 3, NT])
        shift = sb("shift", [TP, 3, NT])
        gain = sb("gain", [TP, NT])
        xc = [sb(f"xc{d}", [128, 2, TC]) for d in range(2)]
        gate = [sb(f"gate{d}", [128, 2, TC]) for d in range(2)]
        delta = [sb(f"delta{d}", [128, 2, TC]) for d in range(2)]
        u = [sb(f"u{d}", [128, 2, TC]) for d in range(2)]
        parts = [sb(f"parts{d}", [K2, TC], BF16) for d in range(2)]
        c_all = [sb(f"c_all{d}", [128, NS, TC]) for d in range(2)]
        cwb = c_all[1][:].rearrange("p n t -> p (n t)")[:, 0:2 * TAPS * DI].rearrange("p (d k e) -> p d k e", d=2, k=TAPS)
        yg = [sb(f"yg{d}", [128, 2, TC]) for d in range(2)]
        dbl = sb("dbl", [XR, TC])
        rest = sb("rest", [K2, TC])
        mid = sb("mid", [K2, TC], BF16)
        e_neg = sb("e_neg", [128, 2, TC])
        e_one = sb("e_one", [128, 2, TC])
        log1 = sb("log1", [128, 2, TC])
        relu = sb("relu", [128, 2, TC])
        da = [sb(f"da{j}", [128, 2, SC, T]) for j in range(RING)]
        h = [sb(f"hc{j}", [128, UC]) for j in range(RING)]
        yv = sb("yv", [128, 2, TC])
        s = sb("s", [TP, NT, DM])
        out_sb = sb("out_sb", [TP, NT, DM])

        g_ps = [ctx.enter_context(nc.psum_tensor(f"g_ps{j}", [128, 2 * BANK], F32)) for j in range(2)]
        y_ps = [ctx.enter_context(nc.psum_tensor(f"y_ps{j}", [128, BANK], F32)) for j in range(2)]
        m_ps = [ctx.enter_context(nc.psum_tensor(f"m_ps{j}", [128, BANK], F32)) for j in range(2)]

        loaded = sem("loaded")
        setup_dve = sem("setup_dve")
        setup_act = sem("setup_act")
        setup_pool = sem("setup_pool")
        x_loaded = sem("x_loaded")
        job_filled = sem("job_filled")
        job_drained = sem("job_drained")
        h0_ready = sem("h0_ready")
        ln_step = [sem(f"ln_step{n}") for n in range(3)]
        ln_pow = [sem(f"ln_pow{n}") for n in range(3)]
        ln_ready = [sem(f"ln_ready{n}") for n in range(3)]
        z_ready = sem("z_ready")
        kept = sem("kept")
        split_step = sem("split_step")
        split_done = sem("split_done")
        exp_ready = sem("exp_ready")
        one_ready = sem("one_ready")
        sp_ready = sem("sp_ready")
        log_ready = sem("log_ready")
        sp_step = sem("sp_step")
        delta_ready = sem("delta_ready")
        u_ready = sem("u_ready")
        b_filled = sem("b_filled")
        dbx_ready = sem("dbx_ready")
        da_ready = sem("da_ready")
        scanned = sem("scanned")
        hc_ready = sem("hc_ready")
        summed = sem("summed")
        y_read = sem("y_read")
        yg_ready = sem("yg_ready")
        s_ready = sem("s_ready")
        q_ready = sem("q_ready")
        h1_step = sem("h1_step")
        h1_ready = sem("h1_ready")
        out_ready = sem("out_ready")
        out_stored = sem("out_stored")

        block = ctx.enter_context(nc.Block())
        out_v = out.rearrange("(c j p) n -> c p j n", j=NT, p=TP)
        x_v = x_t.rearrange("h p (c t) -> c p h t", t=TC)
        loads = [(tokw[:], tok_w.rearrange("h p n -> p h n")), (tokb[:], tok_b.partition_broadcast(TP)),
                 (lng[:], ln_g.partition_broadcast(TP)), (lnb[:], ln_b.partition_broadcast(TP)),
                 (ident[:], eye), (eyes[:], eye3)]
        for d, (in_w, conv_w, conv_b, xproj_w, dt_w, dt_b, a_log, d_skip, out_w) in enumerate(dirs):
            loads += [(inw[d][:], in_w), (cwb[:, d], conv_w.partition_broadcast(128)), (convb[:, d], conv_b),
                      (xpw[:, d], xproj_w), (dtw[DT0:XR, d], dt_w), (dtb[:, d], dt_b), (a_neg[:, d], a_log),
                      (dskip[:, d], d_skip), (outw[:, d], out_w)]
        LOADED = 16 * len(loads)
        SETUP_DVE = 1 + RING + 2 + 1 + 2 * TAPS + 1

        def chunks(eng, chunk):
            chunk(0)
            chunk(1)
            with eng.Fori(2, NCH - 1) as i:
                chunk(i)
            chunk(NCH - 1)

        @block.sync
        def _(sp):
            sp.dma_start(xin[:], x_v[0]).then_inc(x_loaded, 16)
            for dst, src in loads:
                sp.dma_start(dst, src).then_inc(loaded, 16)

            def fetch(c):
                sp.wait_ge(job_filled, job(c - 1, "tokens"))
                sp.dma_start(xin[:], x_v[c]).then_inc(x_loaded, 16)

            def store(c):
                sp.wait_ge(out_ready, c + 1)
                sp.dma_start(out_v[c], out_sb[:]).then_inc(out_stored, 16)

            fetch(1)
            fetch(2)
            with sp.Fori(1, NCH - 2) as i:
                store(i - 1)
                fetch(i + 2)
            for c in range(NCH - 3, NCH):
                store(c)
            sp.wait_ge(out_stored, 16 * NCH)

        @block.tensor
        def _(pe):
            pe.wait_ge(loaded, LOADED)

            def bank(c, what, d=0, n=0):
                if late(job(c, what, d, n) - 2):
                    pe.wait_ge(job_drained, job(c, what, d, n) - 2)
                return m_ps[bank_of(c, what, d, n)]

            def tokens(c):
                pe.wait_ge(x_loaded, 16 * (c + 1))
                m = bank(c, "tokens")
                for j in range(NT):
                    for half_k in range(2):
                        mm = pe.matmul(m[0:TP, j * DM:(j + 1) * DM], xin[:, half_k, j * TP:(j + 1) * TP],
                                       tokw[:, half_k, :], start=half_k == 0, stop=half_k == 1)
                mm.then_inc(job_filled, 1)

            def turn(c):
                pe.wait_ge(z_ready, c + 1)
                m = bank(c, "turn")
                for j in range(NT):
                    mm = pe.transpose(m[:, j * TP:(j + 1) * TP], z[:, j, :], ident[0:TP, 0:TP])
                mm.then_inc(job_filled, 1)

            def columns(m):
                return m[:, 0:TC].rearrange("p (s t) -> p s t", s=SC)

            def conv(c, d, db):
                pe.wait_ge(job_drained, job(c, "turn"))
                m = bank(c, "conv", d, db)
                for k in range(TAPS):
                    moving = zt[:, :, k:k + T] if d == 0 else zt[:, :, TW - 1 - k:TW - 1 - k - T:-1]
                    mm = pe.matmul(columns(m), convw[d][:, k, db * 128:(db + 1) * 128], moving,
                                   start=k == 0, stop=k == TAPS - 1)
                mm.then_inc(job_filled, 1)

            def gates(c, d, db):
                m = bank(c, "gate", d, db)
                moving = zt[:, :, PAD:PAD + T] if d == 0 else zt[:, :, PAD + T - 1:PAD - 1:-1]
                pe.matmul(columns(m), inw[d][:, DI + db * 128:DI + (db + 1) * 128], moving,
                          start=True, stop=True).then_inc(job_filled, 1)

            def xproj(c, d):
                pe.wait_ge(job_drained, job(c, "conv", d, 1))
                m = bank(c, "xproj", d)
                for db in range(2):
                    mm = pe.matmul(m[0:XR, 0:TC], xpw[:, d, db, :], xc[d][:, db, :], start=db == 0, stop=db == 1)
                mm.then_inc(job_filled, 1)

            def dt_proj(c, d, db):
                pe.wait_ge(job_drained, job(c, "xproj", d))
                m = bank(c, "dt", d, db)
                pe.matmul(m[:, 0:TC], dtw[DT0:XR, d, db * 128:(db + 1) * 128], dbl[DT0:XR, :],
                          start=True, stop=True).then_inc(job_filled, 1)

            def spread_c(c, d, n):
                if n == 0:
                    pe.wait_ge(split_done, 2 * c + (d + 1))
                m = bank(c, "c", d, n)
                pe.matmul(m[:, 0:TC], pick[:, NS + n, :], parts[d][:], start=True, stop=True).then_inc(job_filled, 1)

            def out_proj(c, part):
                pe.wait_ge(yg_ready, 4 * (c + 1))
                m = bank(c, "tail", 0, part)
                for j in range(2):
                    at = (2 * part + j) * TP
                    for n in range(4):
                        mm = pe.matmul(m[0:TP, j * DM:(j + 1) * DM], yg[n // 2][:, n % 2, at:at + TP],
                                       outw[:, n // 2, n % 2, :], start=n == 0, stop=n == 3)
                mm.then_inc(job_filled, 1)

            def spread_b(unit):
                i, d, k = unit
                n = nth(*unit)
                if k == 0:
                    pe.wait_ge(split_done, 2 * i + (d + 1))
                if late(n - 1):
                    pe.wait_ge(scanned, n - 1)
                g, r = g_ps[k % 2], 2 * (k % PAIRS)
                edge = BANK - TC
                pe.matmul(g[:, 0:TC], pick[:, r, :], parts[d][:], start=True, stop=True)
                pe.matmul(g[:, TC:BANK], pick[:, r + 1, :], parts[d][:, 0:edge], start=True, stop=True)
                pe.matmul(g[:, BANK:UC], pick[:, r + 1, :], parts[d][:, edge:TC],
                          start=True, stop=True).then_inc(b_filled, 1)

            def add_up(unit):
                i, d, k = unit
                db, r = k // PAIRS, k % PAIRS
                if r == 0:
                    if late(4 * i + (2 * d + db - 1)):
                        pe.wait_ge(y_read, 4 * i + (2 * d + db - 1))
                pe.wait_ge(hc_ready, nth(*unit) + 1)
                for j in range(2):
                    mm = pe.matmul(y_ps[db][:, 0:TC], ident[:], h[k % RING][:, j * TC:(j + 1) * TC],
                                   start=r == 0 and j == 0, stop=r == PAIRS - 1 and j == 1)
                mm.then_inc(summed, 1)

            pe.wait_ge(setup_dve, SETUP_DVE)
            tokens(0)
            turn(0)
            for db in range(2):
                conv(0, 0, db)
            for db in range(2):
                gates(0, 0, db)
            xproj(0, 0)
            for db in range(2):
                dt_proj(0, 0, db)
            for n in range(NS):
                spread_c(0, 0, n)
            spread_b((0, 0, 0))

            def chunk(i):
                for d in range(2):
                    fc, fd = (i, 1) if d == 0 else (i + 1, 0)
                    front = d == 0 or not (isinstance(i, int) and i == NCH - 1)
                    tail = d == 0 and not (isinstance(i, int) and i == 0)
                    for k in range(UNITS):
                        if front:
                            if d == 1 and k == 0:
                                tokens(fc)
                            if d == 1 and k == 3:
                                turn(fc)
                            if k in (4, 5):
                                conv(fc, fd, k - 4)
                            if k == 6:
                                gates(fc, fd, 0)
                                gates(fc, fd, 1)
                            if k == 7:
                                xproj(fc, fd)
                        if tail and k in (7, 8):
                            out_proj(i - 1, k - 7)
                        if front:
                            if k == 8:
                                dt_proj(fc, fd, 0)
                                dt_proj(fc, fd, 1)
                            for n in range(*C_SLOTS.get(k, (0, 0))):
                                spread_c(fc, fd, n)
                        later, before = ahead(i, d, k, 1), back(i, d, k, 2)
                        if later:
                            spread_b(later)
                        if before:
                            add_up(before)

            chunks(pe, chunk)
            for k in range(UNITS - 2, UNITS):
                add_up((NCH - 1, 1, k))
            out_proj(NCH - 1, 0)
            out_proj(NCH - 1, 1)

        @block.scalar
        def _(act):
            act.wait_ge(loaded, LOADED)
            act.activation(a_neg[:], a_neg[:], ACT.Exp).then_inc(setup_act, 1)

            def bank(c, what, d=0, n=0):
                act.wait_ge(job_filled, job(c, what, d, n))
                return m_ps[bank_of(c, what, d, n)]

            def tokens(c):
                if late(2 * c):
                    act.wait_ge(kept, 2 * c)
                m = bank(c, "tokens")
                act.activation(h0[:].rearrange("p j n -> p (j n)"), m[0:TP, :], ACT.Copy).then_inc(job_drained, 1)

            def norm_z(c):
                act.wait_ge(ln_ready[0], c + 1)
                for j in range(NT):
                    op = act.activation(z[:, j, :], h0[:, j, :], ACT.Identity, bias=shift[:, 0, j:j + 1],
                                        scale=rstd[:, 0, j:j + 1])
                op.then_inc(z_ready, 1)

            def turned(c):
                m = bank(c, "turn")
                act.activation(zt[:, :, PAD:PAD + T], m[:, 0:TC].rearrange("p (s t) -> p s t", s=SC),
                               ACT.Copy).then_inc(job_drained, 1)

            def silus(c, d):
                if late(4 * c + (2 * d - 2)):
                    act.wait_ge(y_read, 4 * c + (2 * d - 2))
                for db in range(2):
                    m = bank(c, "conv", d, db)
                    act.activation(xc[d][:, db, :], m[:, 0:TC], ACT.Silu,
                                   bias=convb[:, d, db:db + 1]).then_inc(job_drained, 1)
                if late(4 * c + (2 * d - 2)):
                    act.wait_ge(yg_ready, 4 * c + (2 * d - 2))
                for db in range(2):
                    m = bank(c, "gate", d, db)
                    act.activation(gate[d][:, db, :], m[:, 0:TC], ACT.Silu).then_inc(job_drained, 1)

            def xproj(c, d):
                if late(2 * c + d):
                    act.wait_ge(split_done, 2 * c + d)
                if late(nth(c, d, 0) - UNITS):
                    act.wait_ge(b_filled, nth(c, d, 0) - UNITS)
                m = bank(c, "xproj", d)
                act.activation(dbl[:], m[0:XR, 0:TC], ACT.Copy)
                act.activation(parts[d][:], m[0:K2, 0:TC], ACT.Copy).then_inc(job_drained, 1)

            def out_half(c, part):
                if late(c):
                    act.wait_ge(out_ready, c)
                m = bank(c, "tail", 0, part)
                act.activation(s[:, 2 * part:2 * part + 2, :].rearrange("p j n -> p (j n)"), m[0:TP, 0:2 * DM],
                               ACT.Copy, scale=0.5).then_inc(job_drained, 1)

            def softplus(c, d):
                if late(2 * c + d):
                    act.wait_ge(u_ready, 2 * c + d)
                for db in range(2):
                    m = bank(c, "dt", d, db)
                    act.activation(e_neg[:, db, :], m[:, 0:TC], ACT.Abs, bias=dtb[:, d, db:db + 1])
                    act.activation(relu[:, db, :], m[:, 0:TC], ACT.Relu,
                                   bias=dtb[:, d, db:db + 1]).then_inc(job_drained, 1)
                act.wait_ge(job_drained, job(c, "dt", d, 1))
                act.activation(e_neg[:], e_neg[:], ACT.Exp, scale=-1.0).then_inc(exp_ready, 1)
                act.wait_ge(exp_ready, 2 * c + (d + 1))
                act.activation(e_one[:], e_neg[:], ACT.Identity, bias=ones[:, 0:1]).then_inc(one_ready, 1)
                act.activation(log1[:], e_neg[:], ACT.Ln, bias=ones[:, 0:1])
                act.wait_ge(one_ready, 2 * c + (d + 1))
                act.activation(e_one[:], e_one[:], ACT.Identity, bias=ones[:, 1:2]).then_inc(sp_ready, 1)

            def spread_c(c, d, n):
                if late(nth(c, d, 0) - 2 * UNITS + (PAIRS + n // 2 + 1)):
                    act.wait_ge(hc_ready, nth(c, d, 0) - 2 * UNITS + (PAIRS + n // 2 + 1))
                m = bank(c, "c", d, n)
                act.activation(c_all[d][:, n, :], m[:, 0:TC], ACT.Copy).then_inc(job_drained, 1)

            def norm_q(c):
                act.wait_ge(ln_ready[1], c + 1)
                for j in range(NT):
                    op = act.activation(s[:, j, :], s[:, j, :], ACT.Identity, bias=shift[:, 1, j:j + 1],
                                        scale=rstd[:, 1, j:j + 1])
                op.then_inc(q_ready, 1)

            def norm_out(c):
                if late(16 * c):
                    act.wait_ge(out_stored, 16 * c)
                act.wait_ge(ln_ready[2], c + 1)
                for j in range(NT):
                    op = act.activation(out_sb[:, j, :], s[:, j, :], ACT.Identity, bias=shift[:, 2, j:j + 1],
                                        scale=gain[:, j:j + 1])
                op.then_inc(out_ready, 1)

            def decay(unit):
                i, d, k = unit
                if k == 0:
                    act.wait_ge(delta_ready, 2 * i + (d + 1))
                if late(nth(*unit) - (RING - 1)):
                    act.wait_ge(scanned, nth(*unit) - (RING - 1))
                db, r = k // PAIRS, 2 * (k % PAIRS)
                steps = delta[d][:, db, :].rearrange("p (s t) -> p s t", s=SC)[:, :, 1:T]
                for j in range(2):
                    op = act.activation(da[k % RING][:, j, :, 1:T], steps, ACT.Exp,
                                        scale=a_neg[:, d, db, r + j:r + j + 1])
                op.then_inc(da_ready, 1)

            act.wait_ge(setup_dve, SETUP_DVE)
            tokens(0)
            norm_z(0)
            turned(0)
            silus(0, 0)
            xproj(0, 0)
            softplus(0, 0)
            for n in range(NS):
                spread_c(0, 0, n)
            for k in range(2):
                decay((0, 0, k))

            def chunk(i):
                for d in range(2):
                    fc, fd = (i, 1) if d == 0 else (i + 1, 0)
                    front = d == 0 or not (isinstance(i, int) and i == NCH - 1)
                    tail = d == 0 and not (isinstance(i, int) and i == 0)
                    for k in range(UNITS):
                        later = ahead(i, d, k, 2)
                        if later:
                            decay(later)
                        if front:
                            if d == 1 and k == 0:
                                tokens(fc)
                            if d == 1 and k == 2:
                                norm_z(fc)
                            if d == 1 and k == 3:
                                turned(fc)
                            if k == 6:
                                silus(fc, fd)
                            if k == 7:
                                xproj(fc, fd)
                        if tail and k in (7, 8):
                            out_half(i - 1, k - 7)
                        if front:
                            if k == 8:
                                softplus(fc, fd)
                            for n in range(*C_SLOTS.get(k, (0, 0))):
                                spread_c(fc, fd, n)
                        if tail and k == 11:
                            norm_q(i - 1)
                        if tail and k == 15:
                            norm_out(i - 1)

            chunks(act, chunk)
            out_half(NCH - 1, 0)
            out_half(NCH - 1, 1)
            norm_q(NCH - 1)
            norm_out(NCH - 1)

        @block.gpsimd
        def _(pool):
            pool.memset(half[:], -0.5).then_inc(setup_pool, 1)
            pool.wait_ge(loaded, LOADED)

            def spread(row):
                return row[:].unsqueeze(1).broadcast_to([TP, NT, DM])

            def add_bias(c):
                pool.wait_ge(job_drained, job(c, "tokens"))
                pool.tensor_tensor(h0[:], h0[:], spread(tokb), ALU.add).then_inc(h0_ready, 1)

            def power(n, c):
                pool.wait_ge(ln_step[n], 3 * c + 3)
                pool.tensor_tensor(rstd[:, n, :], vareps[:, n, :], half[:], ALU.pow).then_inc(ln_pow[n], 1)

            def keep(c):
                if late(c):
                    pool.wait_ge(h1_ready, c)
                pool.wait_ge(z_ready, c + 1)
                pool.tensor_tensor(h0b_kept[:], h0[:], spread(lnb), ALU.add).then_inc(kept, 1)
                pool.tensor_copy(z_kept[:], z[:]).then_inc(kept, 1)

            def split(c, d):
                step = 3 * (2 * c + d)
                pool.wait_ge(job_drained, job(c, "xproj", d))
                pool.tensor_tensor(rest[64:96, :], dbl[64:96, :], parts[d][64:96, :],
                                   ALU.subtract).then_inc(split_step, 1)
                pool.wait_ge(split_step, step + 1)
                pool.tensor_tensor(mid[64:96, :], dbl[64:96, :], parts[d][64:96, :],
                                   ALU.subtract).then_inc(split_step, 1)
                pool.wait_ge(split_step, step + 2)
                pool.tensor_tensor(parts[d][32:64, :], dbl[32:64, :], parts[d][32:64, :],
                                   ALU.subtract).then_inc(split_step, 1)
                pool.wait_ge(split_step, step + 3)
                pool.tensor_tensor(parts[d][64:96, :], rest[64:96, :], mid[64:96, :],
                                   ALU.subtract).then_inc(split_done, 1)
                pool.wait_ge(split_done, 2 * c + (d + 1))

            def softplus(c, d):
                step = 2 * (2 * c + d)
                pool.wait_ge(log_ready, 2 * c + (d + 1))
                pool.tensor_tensor(e_one[:], e_one[:], e_neg[:], ALU.subtract).then_inc(sp_step, 1)
                pool.wait_ge(sp_step, step + 1)
                pool.tensor_tensor(log1[:], log1[:], e_one[:], ALU.subtract).then_inc(sp_step, 1)
                pool.wait_ge(sp_step, step + 2)
                if late(nth(c, d, 0) - UNITS):
                    pool.wait_ge(da_ready, nth(c, d, 0) - UNITS)
                pool.tensor_tensor(delta[d][:], log1[:], relu[:], ALU.add).then_inc(delta_ready, 1)
                pool.wait_ge(delta_ready, 2 * c + (d + 1))
                if late(nth(c, d, 0) - UNITS):
                    pool.wait_ge(dbx_ready, nth(c, d, 0) - UNITS)
                pool.tensor_tensor(u[d][:], delta[d][:], xc[d][:], ALU.mult).then_inc(u_ready, 1)

            def times_c(unit):
                i, d, k = unit
                r = 2 * (k % PAIRS)
                if k < PAIRS:
                    pool.wait_ge(job_drained, job(i, "c", d, r + 1))
                pool.wait_ge(scanned, nth(*unit) + 1)
                pool.tensor_tensor(h[k % RING][:], h[k % RING][:],
                                   c_all[d][:, r:r + 2, :].rearrange("p n t -> p (n t)"), ALU.mult)\
                    .then_inc(hc_ready, 1)

            def gated(i, d, db):
                pool.wait_ge(y_read, 4 * i + (2 * d + db + 1))
                pool.wait_ge(job_drained, job(i, "gate", d, db))
                if not (isinstance(i, int) and i == 0):
                    pool.wait_ge(job_filled, job(i - 1, "tail", 0, 1))
                dst = yg[d][:, db, :].rearrange("p (s t) -> p s t", s=SC)
                dst = dst if d == 0 else dst[:, :, ::-1]
                pool.tensor_tensor(dst, yv[:, db, :].rearrange("p (s t) -> p s t", s=SC),
                                   gate[d][:, db, :].rearrange("p (s t) -> p s t", s=SC),
                                   ALU.mult).then_inc(yg_ready, 1)

            def add_z(c):
                pool.wait_ge(job_drained, job(c, "tail", 0, 1))
                pool.wait_ge(kept, 2 * (c + 1))
                pool.tensor_tensor(s[:], s[:], z_kept[:], ALU.add).then_inc(s_ready, 1)

            def residual(c):
                pool.wait_ge(q_ready, c + 1)
                pool.tensor_tensor(s[:], s[:], spread(lng), ALU.mult).then_inc(h1_step, 1)
                pool.wait_ge(h1_step, c + 1)
                pool.tensor_tensor(s[:], s[:], h0b_kept[:], ALU.add).then_inc(h1_ready, 1)

            pool.wait_ge(setup_pool, 1)
            add_bias(0)
            power(0, 0)
            pool.wait_ge(ln_pow[0], 1)
            split(0, 0)
            softplus(0, 0)

            def chunk(i):
                for d in range(2):
                    fc, fd = (i, 1) if d == 0 else (i + 1, 0)
                    front = d == 0 or not (isinstance(i, int) and i == NCH - 1)
                    tail = d == 0 and not (isinstance(i, int) and i == 0)
                    for k in range(UNITS):
                        before = back(i, d, k, 1)
                        if before:
                            times_c(before)
                        if k == 2 and back(i, d, k, 3):
                            gated(*back(i, d, k, 3)[:2], 1)
                        if k == 10:
                            gated(i, d, 0)
                        if front:
                            if d == 1 and k == 0:
                                add_bias(fc)
                            if d == 1 and k == 1:
                                power(0, fc)
                            if k == 7:
                                pool.wait_ge(hc_ready, nth(i, d, k))
                                split(fc, fd)
                            if k == 9:
                                softplus(fc, fd)
                        if tail:
                            if k == 8:
                                add_z(i - 1)
                            if k == 10:
                                power(1, i - 1)
                            if k == 12:
                                residual(i - 1)
                            if k == 13:
                                power(2, i - 1)
                        if d == 0 and k == 14:
                            keep(i)

            chunks(pool, chunk)
            times_c((NCH - 1, 1, UNITS - 1))
            gated(NCH - 1, 1, 1)
            add_z(NCH - 1)
            power(1, NCH - 1)
            residual(NCH - 1)
            power(2, NCH - 1)

        @block.vector
        def _(dve):
            dve.memset(zt[:], 0.0).then_inc(setup_dve, 1)
            for j in range(RING):
                dve.memset(da[j][:], 0.0).then_inc(setup_dve, 1)
            dve.memset(ones[:, 0:1], 1.0).then_inc(setup_dve, 1)
            dve.memset(ones[:, 1:2], -1.0).then_inc(setup_dve, 1)
            dve.wait_ge(loaded, LOADED)
            dve.tensor_copy(pick[:], eyes[:].unsqueeze(2).broadcast_to([K2, 32, 128])).then_inc(setup_dve, 1)
            for d in range(2):
                for k in range(TAPS):
                    dve.tensor_tensor(convw[d][:, k, :], inw[d][:, 0:DI], cwb[:, d, k, :],
                                      ALU.mult).then_inc(setup_dve, 1)
            dve.wait_ge(setup_act, 1)
            dve.tensor_scalar(a_neg[:], a_neg[:], -1.0, None, ALU.mult).then_inc(setup_dve, 1)

            def statistics(n, src, c):
                for j in range(NT):
                    op = dve.bn_stats(stats[:, n, j, :], src[:, j, :])
                op.then_inc(ln_step[n], 1)
                dve.wait_ge(ln_step[n], 3 * c + 1)
                dve.memset(vareps[:, n, :], EPS)
                for j in range(NT):
                    op = dve.bn_aggr(meanvar[:, n, j, :], stats[:, n, j, :])
                op.then_inc(ln_step[n], 1)
                dve.wait_ge(ln_step[n], 3 * c + 2)
                dve.tensor_tensor(vareps[:, n, :], vareps[:, n, :], meanvar[:, n, :, 1],
                                  ALU.add).then_inc(ln_step[n], 1)

            def shifts(n, c):
                dve.wait_ge(ln_pow[n], c + 1)
                if n == 2:
                    dve.tensor_scalar(gain[:], rstd[:, n, :], 1.0, None, ALU.add)
                dve.scalar_tensor_tensor(out=shift[:, n, :], in0=meanvar[:, n, :, 0], scalar=-1.0,
                                         in1=rstd[:, n, :], op0=ALU.mult, op1=ALU.mult).then_inc(ln_ready[n], 1)

            def times_b(unit):
                i, d, k = unit
                if k == 0:
                    dve.wait_ge(u_ready, 2 * i + (d + 1))
                dve.wait_ge(b_filled, nth(*unit) + 1)
                g = g_ps[k % 2][:, 0:UC].rearrange("p (n t) -> p n t", n=2)
                dve.tensor_tensor(g, u[d][:, k // PAIRS, :].unsqueeze(1).broadcast_to([128, 2, TC]), g,
                                  ALU.mult).then_inc(dbx_ready, 1)

            def scan(unit):
                i, d, k = unit
                n = nth(*unit)
                dve.wait_ge(da_ready, n + 1)
                if late(n - (RING - 1)):
                    dve.wait_ge(summed, n - (RING - 1))
                dve.wait_ge(dbx_ready, n + 1)
                dve.tensor_tensor_scan(h[k % RING][:], da[k % RING][:].rearrange("p n s t -> p (n s t)"),
                                       g_ps[k % 2][:, 0:UC], 0.0, ALU.mult, ALU.add).then_inc(scanned, 1)

            def skip(i, d, db):
                at = 4 * i + (2 * d + db)
                dve.wait_ge(summed, nth(i, d, PAIRS * (db + 1)))
                if late(at - 1):
                    dve.wait_ge(yg_ready, at - 1)
                dve.scalar_tensor_tensor(out=yv[:, db, :], in0=xc[d][:, db, :], scalar=dskip[:, d, db:db + 1],
                                         in1=y_ps[db][:, 0:TC], op0=ALU.mult, op1=ALU.add).then_inc(y_read, 1)

            def log_above(c, d):
                dve.wait_ge(sp_ready, 2 * c + (d + 1))
                dve.scalar_tensor_tensor(out=log1[:], in0=e_one[:], scalar=0.0, in1=log1[:],
                                         op0=ALU.is_gt, op1=ALU.mult).then_inc(log_ready, 1)

            dve.wait_ge(h0_ready, 1)
            statistics(0, h0, 0)
            shifts(0, 0)
            log_above(0, 0)

            def chunk(i):
                for d in range(2):
                    fc, fd = (i, 1) if d == 0 else (i + 1, 0)
                    front = d == 0 or not (isinstance(i, int) and i == NCH - 1)
                    tail = d == 0 and not (isinstance(i, int) and i == 0)
                    for k in range(UNITS):
                        times_b((i, d, k))
                        scan((i, d, k))
                        if k == 2 and back(i, d, k, 3):
                            skip(*back(i, d, k, 3)[:2], 1)
                        if k == 10:
                            skip(i, d, 0)
                        if front and k == 9:
                            log_above(fc, fd)
                        if front and d == 1 and k == 1:
                            dve.wait_ge(h0_ready, i + 2)
                            dve.wait_ge(z_ready, i + 1)
                            statistics(0, h0, i + 1)
                        if front and d == 1 and k == 2:
                            shifts(0, i + 1)
                        if tail and k == 9:
                            dve.wait_ge(s_ready, i)
                            if late(i - 1):
                                dve.wait_ge(q_ready, i - 1)
                            statistics(1, s, i - 1)
                        if tail and k == 10:
                            shifts(1, i - 1)
                        if tail and k == 12:
                            dve.wait_ge(h1_ready, i)
                            if late(i - 1):
                                dve.wait_ge(out_ready, i - 1)
                            statistics(2, s, i - 1)
                        if tail and k == 14:
                            shifts(2, i - 1)

            chunks(dve, chunk)
            skip(NCH - 1, 1, 1)
            for n, ready in ((1, s_ready), (2, h1_ready)):
                dve.wait_ge(ready, NCH)
                dve.wait_ge((q_ready, out_ready)[n - 1], NCH - 1)
                statistics(n, s, NCH - 1)
                shifts(n, NCH - 1)


def kernel(x, L0_tok_weight, L0_tok_bias, L0_attn_ln_g, L0_attn_ln_b, L0_ffn_W, L0_ffn_b, **attn):
    import numpy as np
    import concourse.bacc as bacc
    from concourse.bass_utils import run_bass_kernel_spmd

    nc = bacc.Bacc("TRN2", target_bir_lowering=False, num_devices=1)
    arrays = {}

    def given(name, a):
        arrays[name] = np.ascontiguousarray(a)
        return nc.dram_tensor(name, arrays[name].shape, mybir.dt.from_np(arrays[name].dtype), kind="ExternalInput").ap()

    def halves(a):
        return np.moveaxis(np.asarray(a).reshape(2, 128, *np.asarray(a).shape[1:]), 0, 1)

    tokens = np.asarray(x).reshape(SEQS * T, 2 * K2)
    x_t = given("x_t", tokens.T.reshape(2, K2, SEQS * T))
    tok_w = given("tok_w", np.asarray(L0_tok_weight).T.reshape(2, K2, DM))
    tok_b = given("tok_b", np.asarray(L0_tok_bias).reshape(DM))
    dirs = []
    for d in "fb":
        w = {k[len("L0_attn_f_"):]: np.asarray(v) for k, v in attn.items() if k.startswith(f"L0_attn_{d}_")}
        dt_rows, bc_rows = w["x_proj"][:RANK], w["x_proj"][RANK:]
        rows = np.concatenate([bc_rows, bc_rows, bc_rows, dt_rows])
        dirs.append((given(f"{d}_in_w", w["in_proj"].T), given(f"{d}_conv_w", w["conv_w"].T),
                     given(f"{d}_conv_b", halves(w["conv_b"])), given(f"{d}_xproj_w", halves(rows.T)),
                     given(f"{d}_dt_w", w["dt_w"].T), given(f"{d}_dt_b", halves(w["dt_b"])),
                     given(f"{d}_a_log", halves(w["A_log"])), given(f"{d}_d_skip", halves(w["Dv"])),
                     given(f"{d}_out_w", halves(w["out_proj"].T))))
    ln_g, ln_b = given("ln_g", L0_attn_ln_g), given("ln_b", L0_attn_ln_b)
    eye = given("eye", np.eye(128, dtype=np.float32))
    eye3 = given("eye3", np.tile(np.eye(32, dtype=np.float32), (3, 1)))
    out = nc.dram_tensor("out", (SEQS * T, DM), F32, kind="ExternalOutput").ap()
    audio_tower_kernel(nc, x_t, tok_w, tok_b, dirs, ln_g, ln_b, eye, eye3, out)
    r = run_bass_kernel_spmd(nc, [arrays], core_ids=[0])
    return r.results[0]["out"].reshape(SEQS, T, DM)
```

```python
from contextlib import ExitStack

import concourse.bass as bass
from concourse import mybir

F32 = mybir.dt.float32
BF16 = mybir.dt.bfloat16
ALU = mybir.AluOpType
ACT = mybir.ActivationFunctionType

SEQS, T, DM = 64, 250, 128
K2 = 96
DI, NS, RANK = 256, 16, 8
TAPS = 4
SC = 2
TC = SC * T
NCH = SEQS // SC
TP, NT = 125, 4
PAD = TAPS - 1
TW = T + 2 * PAD
PAIRS = NS // 2
UNITS = 2 * PAIRS
UC = 2 * TC
RING = 4
HRING = 8
XR = 3 * 2 * NS + RANK
DT0 = 3 * 2 * NS
BANK = 512
EPS = 1e-5

FRONT = [("conv", 0), ("conv", 1), ("gate", 0), ("gate", 1),
         ("xproj", 0), ("dt", 0), ("split", 1), ("dt", 1), ("split", 2)]
C_SLOT = 10
C_BEFORE = 2 * (UNITS - C_SLOT)
C_FIRST = [("c", n) for n in range(C_BEFORE)]
C_LAST = [("c", n) for n in range(C_BEFORE, NS)]
TAIL = [("tail", 0), ("tail", 1)]
JOBS_AHEAD = 2 + len(FRONT + C_FIRST)

CONV0, CONV1, SILU, XPROJ, SPLIT1, SPLIT2, LOG, SOFTPLUS = 1, 2, 4, 5, 6, 7, 8, 9
TOKENS, STATS_Z, POW_Z, SHIFT_Z, NORM_Z, TURN = 0, 1, 2, 3, 5, 9
TAIL_AT, ADD_Z, STATS_Q, POW_Q, SHIFT_Q, NORM_Q = 8, 10, 11, 12, 13, 14
RESIDUAL, STATS_OUT, POW_OUT, SHIFT_OUT, NORM_OUT = 0, 2, 3, 5, 6
KEEP, TAKE = 2, 4
SKIP0, SKIP1 = 11, 3
LAG = 3


def jobs_beside(i, d):
    first, last = isinstance(i, int) and i == 0, isinstance(i, int) and i == NCH - 1
    if d == 1:
        return C_LAST + ([] if last else FRONT + C_FIRST)
    return (C_LAST[:2] + ([] if last else [("tokens", 0)]) + C_LAST[2:] + FRONT + ([] if first else TAIL)
            + ([] if last else [("turn", 0)]) + C_FIRST)


JOBS_CHUNK = len(jobs_beside(1, 0) + jobs_beside(1, 1))


def jobs_before(i, d=0):
    if d == 1:
        return jobs_before(i) + len(jobs_beside(i, 0))
    if isinstance(i, int) and i == 0:
        return JOBS_AHEAD
    if isinstance(i, int) and i == NCH:
        return jobs_before(NCH - 1, 1) + len(jobs_beside(NCH - 1, 1))
    return JOBS_CHUNK * i + (JOBS_AHEAD - len(TAIL))


def job(c, what, d=0, n=0):
    if what == "tail":
        if isinstance(c, int) and c == NCH - 1:
            return jobs_before(NCH) + (n + 1)
        step = (c + 1, 0)
    elif what in ("tokens", "turn"):
        step = (c - 1, 0)
    elif what == "c" and n >= C_BEFORE:
        step = (c, d)
    else:
        step = (c - 1, 1) if d == 0 else (c, 0)
    if isinstance(step[0], int) and step[0] < 0:
        return ([("tokens", 0), ("turn", 0)] + FRONT + C_FIRST).index((what, n)) + 1
    return jobs_before(*step) + (jobs_beside(*step).index((what, n)) + 1)


def bank_of(c, what, d=0, n=0):
    return (job(c if isinstance(c, int) else 3, what, d, n) - 1) % 2


def back(i, d, k, by):
    k -= by
    if k < 0:
        k, d = k + UNITS, d - 1
    if d < 0:
        d, i = d + 2, i - 1
    return None if isinstance(i, int) and i < 0 else (i, d, k)


def ahead(i, d, k, by):
    k += by
    if k >= UNITS:
        k, d = k - UNITS, d + 1
    if d > 1:
        d, i = d - 2, i + 1
    return None if isinstance(i, int) and i >= NCH else (i, d, k)


def nth(i, d, k):
    return 2 * UNITS * i + (UNITS * d + k)


def late(count):
    return not isinstance(count, int) or count > 0


def audio_tower_kernel(nc, x_t, tok_w, tok_b, dirs, ln_g, ln_b, eye, eye3, minus_eye, out):
    with ExitStack() as ctx:
        def sb(name, shape, dt=F32):
            return ctx.enter_context(nc.sbuf_tensor(name, shape, dt))

        def sem(name):
            return ctx.enter_context(nc.semaphore(name))

        tokw = sb("tokw", [K2 + 1, 2, DM])
        lng = sb("lng", [TP, DM])
        lnb = sb("lnb", [TP, DM])
        ident = sb("ident", [128, 128])
        eyes = sb("eyes", [K2, 32])
        minus32 = sb("minus32", [K2, 2, K2])
        pick = sb("pick", [K2, 32, 128], BF16)
        minus = sb("minus", [K2, 2, K2], BF16)
        inw = [sb(f"inw{d}", [128, 2 * DI]) for d in range(2)]
        convw = [sb(f"convw{d}", [128, TAPS, DI]) for d in range(2)]
        convb = sb("convb", [128, 2, 2])
        xpw = sb("xpw", [128, 2, 2, XR])
        dtw = sb("dtw", [XR, 2, DI])
        dtb = sb("dtb", [128, 2, 2])
        a_neg = sb("a_neg", [128, 2, 2, NS])
        dskip = sb("dskip", [128, 2, 2])
        outw = sb("outw", [128, 2, 2, DM])
        half = sb("half", [TP, NT])
        ones = sb("ones", [128, 1])
        xin = sb("xin", [K2 + 1, 2, TC])
        h0 = sb("h0", [TP, NT, DM])
        z = sb("z", [TP, NT, DM])
        zt = sb("zt", [128, SC, TW])
        h0b_now = sb("h0b_now", [TP, NT, DM])
        z_now = sb("z_now", [TP, NT, DM])
        h0b_kept = sb("h0b_kept", [TP, NT, DM])
        z_kept = sb("z_kept", [TP, NT, DM])
        stats = sb("stats", [TP, 3, NT, 6])
        meanvar = sb("meanvar", [TP, 3, NT, 2])
        vareps = sb("vareps", [TP, 3, NT])
        rstd = sb("rstd", [TP, 3, NT])
        shift = sb("shift", [TP, 3, NT])
        gain = sb("gain", [TP, NT])
        xc = [sb(f"xc{d}", [128, 2, TC]) for d in range(2)]
        gate = [sb(f"gate{d}", [128, 2, TC]) for d in range(2)]
        delta = [sb(f"delta{d}", [128, 2, TC]) for d in range(2)]
        u = [sb(f"u{d}", [128, 2, TC]) for d in range(2)]
        parts = [sb(f"parts{d}", [K2, TC], BF16) for d in range(2)]
        c_all = sb("c_all", [128, NS, TC])
        cwb = c_all[:].rearrange("p n t -> p (n t)")[:, 0:2 * TAPS * DI].rearrange("p (d k e) -> p d k e", d=2, k=TAPS)
        yg = [sb(f"yg{d}", [128, 2, TC]) for d in range(2)]
        dbl = sb("dbl", [XR, TC])
        e_neg = sb("e_neg", [128, 2, TC])
        e_one = sb("e_one", [128, 2, TC])
        log1 = sb("log1", [128, 2, TC])
        relu = sb("relu", [128, 2, TC])
        da = [sb(f"da{j}", [128, 2, SC, T]) for j in range(RING)]
        h = [sb(f"hc{j}", [128, UC]) for j in range(HRING)]
        yv = sb("yv", [128, 2, TC])
        s = sb("s", [TP, NT, DM])
        out_sb = sb("out_sb", [TP, NT, DM])

        g_ps = [ctx.enter_context(nc.psum_tensor(f"g_ps{j}", [128, 2 * BANK], F32)) for j in range(2)]
        y_ps = [ctx.enter_context(nc.psum_tensor(f"y_ps{j}", [128, BANK], F32)) for j in range(2)]
        m_ps = [ctx.enter_context(nc.psum_tensor(f"m_ps{j}", [128, BANK], F32)) for j in range(2)]

        loaded = sem("loaded")
        setup_dve = sem("setup_dve")
        setup_act = sem("setup_act")
        setup_pool = sem("setup_pool")
        x_loaded = sem("x_loaded")
        job_filled = sem("job_filled")
        job_drained = sem("job_drained")
        ln_step = [sem(f"ln_step{n}") for n in range(3)]
        ln_pow = [sem(f"ln_pow{n}") for n in range(3)]
        ln_ready = [sem(f"ln_ready{n}") for n in range(3)]
        z_ready = sem("z_ready")
        h0b_taken = sem("h0b_taken")
        z_taken = sem("z_taken")
        kept = sem("kept")
        exp_ready = sem("exp_ready")
        sp_ready = sem("sp_ready")
        masked = sem("masked")
        lost_ready = sem("lost_ready")
        sp_step = sem("sp_step")
        delta_ready = sem("delta_ready")
        u_ready = sem("u_ready")
        b_filled = sem("b_filled")
        dbx_ready = sem("dbx_ready")
        da_ready = sem("da_ready")
        scanned = sem("scanned")
        hc_ready = sem("hc_ready")
        summed = sem("summed")
        y_read = sem("y_read")
        yg_ready = sem("yg_ready")
        s_ready = sem("s_ready")
        q_ready = sem("q_ready")
        h1_step = sem("h1_step")
        h1_ready = sem("h1_ready")
        out_ready = sem("out_ready")
        out_stored = sem("out_stored")

        block = ctx.enter_context(nc.Block())
        out_v = out.rearrange("(c j p) n -> c p j n", j=NT, p=TP)
        x_v = x_t.rearrange("h p (c t) -> c p h t", t=TC)
        loads = [(tokw[0:K2], tok_w.rearrange("h p n -> p h n")), (tokw[K2:K2 + 1, 1, :], tok_b),
                 (lng[:], ln_g.partition_broadcast(TP)), (lnb[:], ln_b.partition_broadcast(TP)),
                 (ident[:], eye), (eyes[:], eye3), (minus32[:], minus_eye)]
        for d, (in_w, conv_w, conv_b, xproj_w, dt_w, dt_b, a_log, d_skip, out_w) in enumerate(dirs):
            loads += [(inw[d][:], in_w), (cwb[:, d], conv_w.partition_broadcast(128)), (convb[:, d], conv_b),
                      (xpw[:, d], xproj_w), (dtw[DT0:XR, d], dt_w), (dtb[:, d], dt_b), (a_neg[:, d], a_log),
                      (dskip[:, d], d_skip), (outw[:, d], out_w)]
        LOADED = 16 * len(loads)
        SETUP_DVE = 1 + RING + 2 + 2 + 2 * TAPS + 1

        def last(i):
            return isinstance(i, int) and i == NCH - 1

        def beside(i, d):
            return d == 0 or not last(i), not (isinstance(i, int) and i == 0) and d == 0, d == 0 and not last(i)

        def c_beside(k, step):
            r = k - C_SLOT + (UNITS if step == 0 else 0)
            return (2 * r, 2 * r + 1) if 0 <= r < PAIRS else ()

        def chunks(eng, chunk):
            chunk(0)
            chunk(1)
            with eng.Fori(2, NCH - 1) as i:
                chunk(i)
            chunk(NCH - 1)

        @block.sync
        def _(sp):
            sp.dma_start(xin[0:K2], x_v[0]).then_inc(x_loaded, 16)
            for dst, src in loads:
                sp.dma_start(dst, src).then_inc(loaded, 16)

            def fetch(c):
                sp.wait_ge(job_filled, job(c - 1, "tokens"))
                sp.dma_start(xin[0:K2], x_v[c]).then_inc(x_loaded, 16)

            def store(c):
                sp.wait_ge(out_ready, c + 1)
                sp.dma_start(out_v[c], out_sb[:]).then_inc(out_stored, 16)

            fetch(1)
            fetch(2)
            with sp.Fori(1, NCH - 2) as i:
                store(i - 1)
                fetch(i + 2)
            for c in range(NCH - 3, NCH):
                store(c)
            sp.wait_ge(out_stored, 16 * NCH)

        @block.tensor
        def _(pe):
            pe.wait_ge(loaded, LOADED)

            def bank(c, what, d=0, n=0):
                if late(job(c, what, d, n) - 2):
                    pe.wait_ge(job_drained, job(c, what, d, n) - 2)
                return m_ps[bank_of(c, what, d, n)]

            def tokens(c):
                pe.wait_ge(x_loaded, 16 * (c + 1))
                m = bank(c, "tokens")
                for j in range(NT):
                    for half_k in range(2):
                        rows = K2 + half_k
                        mm = pe.matmul(m[0:TP, j * DM:(j + 1) * DM], xin[0:rows, half_k, j * TP:(j + 1) * TP],
                                       tokw[0:rows, half_k, :], start=half_k == 0, stop=half_k == 1)
                mm.then_inc(job_filled, 1)

            def turn(c):
                pe.wait_ge(z_ready, c + 1)
                m = bank(c, "turn")
                for j in range(NT):
                    mm = pe.transpose(m[:, j * TP:(j + 1) * TP], z[:, j, :], ident[0:TP, 0:TP])
                mm.then_inc(job_filled, 1)

            def columns(m):
                return m[:, 0:TC].rearrange("p (s t) -> p s t", s=SC)

            def conv(c, d, db):
                pe.wait_ge(job_drained, job(c, "turn"))
                m = bank(c, "conv", d, db)
                for k in range(TAPS):
                    moving = zt[:, :, k:k + T] if d == 0 else zt[:, :, TW - 1 - k:TW - 1 - k - T:-1]
                    mm = pe.matmul(columns(m), convw[d][:, k, db * 128:(db + 1) * 128], moving,
                                   start=k == 0, stop=k == TAPS - 1)
                mm.then_inc(job_filled, 1)

            def gates(c, d, db):
                m = bank(c, "gate", d, db)
                moving = zt[:, :, PAD:PAD + T] if d == 0 else zt[:, :, PAD + T - 1:PAD - 1:-1]
                pe.matmul(columns(m), inw[d][:, DI + db * 128:DI + (db + 1) * 128], moving,
                          start=True, stop=True).then_inc(job_filled, 1)

            def xproj(c, d):
                pe.wait_ge(job_drained, job(c, "conv", d, 1))
                m = bank(c, "xproj", d)
                for db in range(2):
                    mm = pe.matmul(m[0:XR, 0:TC], xpw[:, d, db, :], xc[d][:, db, :], start=db == 0, stop=db == 1)
                mm.then_inc(job_filled, 1)

            def split(c, d, n):
                m = bank(c, "split", d, n)
                pe.matmul(m[0:K2, 0:TC], minus[:, n - 1, :], parts[d][:], start=False, stop=True,
                          skip_group_check=True).then_inc(job_filled, 1)

            def dt_proj(c, d, db):
                pe.wait_ge(job_drained, job(c, "xproj", d))
                m = bank(c, "dt", d, db)
                pe.matmul(m[:, 0:TC], dtw[DT0:XR, d, db * 128:(db + 1) * 128], dbl[DT0:XR, :],
                          start=True, stop=True).then_inc(job_filled, 1)

            def spread_c(c, d, n):
                pe.wait_ge(job_drained, job(c, "split", d, 2))
                m = bank(c, "c", d, n)
                pe.matmul(m[:, 0:TC], pick[:, NS + n, :], parts[d][:], start=True, stop=True).then_inc(job_filled, 1)

            def out_proj(c, part):
                pe.wait_ge(yg_ready, 4 * (c + 1))
                m = bank(c, "tail", 0, part)
                for j in range(2):
                    at = (2 * part + j) * TP
                    for n in range(4):
                        mm = pe.matmul(m[0:TP, j * DM:(j + 1) * DM], yg[n // 2][:, n % 2, at:at + TP],
                                       outw[:, n // 2, n % 2, :], start=n == 0, stop=n == 3)
                mm.then_inc(job_filled, 1)

            def spread_b(unit):
                i, d, k = unit
                n = nth(*unit)
                if k == 0:
                    pe.wait_ge(job_drained, job(i, "split", d, 2))
                if late(n - 1):
                    pe.wait_ge(scanned, n - 1)
                g, r = g_ps[k % 2], 2 * (k % PAIRS)
                edge = BANK - TC
                pe.matmul(g[:, 0:TC], pick[:, r, :], parts[d][:], start=True, stop=True)
                pe.matmul(g[:, TC:BANK], pick[:, r + 1, :], parts[d][:, 0:edge], start=True, stop=True)
                pe.matmul(g[:, BANK:UC], pick[:, r + 1, :], parts[d][:, edge:TC],
                          start=True, stop=True).then_inc(b_filled, 1)

            def add_up(unit):
                i, d, k = unit
                db, r = k // PAIRS, k % PAIRS
                if r == 0:
                    if late(4 * i + (2 * d + db - 1)):
                        pe.wait_ge(y_read, 4 * i + (2 * d + db - 1))
                pe.wait_ge(hc_ready, nth(*unit) + 1)
                for j in range(2):
                    mm = pe.matmul(y_ps[db][:, 0:TC], ident[:], h[k % HRING][:, j * TC:(j + 1) * TC],
                                   start=r == 0 and j == 0, stop=r == PAIRS - 1 and j == 1)
                mm.then_inc(summed, 1)

            pe.wait_ge(setup_dve, SETUP_DVE)
            tokens(0)
            turn(0)
            conv(0, 0, 0)
            conv(0, 0, 1)
            gates(0, 0, 0)
            gates(0, 0, 1)
            xproj(0, 0)
            for db in range(2):
                dt_proj(0, 0, db)
                split(0, 0, db + 1)
            for _, n in C_FIRST:
                spread_c(0, 0, n)
            spread_b((0, 0, 0))

            def chunk(i):
                for d in range(2):
                    fc, fd = (i, 1) if d == 0 else (i + 1, 0)
                    front, tail, more = beside(i, d)
                    for k in range(UNITS):
                        later, before = ahead(i, d, k, 1), back(i, d, k, LAG)
                        if later:
                            spread_b(later)
                        for n in c_beside(k, 0):
                            spread_c(i, d, n)
                        if more and k == TOKENS:
                            tokens(i + 1)
                        if front:
                            if k == CONV0:
                                conv(fc, fd, 0)
                            if k == CONV1:
                                conv(fc, fd, 1)
                            if k == SILU:
                                gates(fc, fd, 0)
                                gates(fc, fd, 1)
                            if k == XPROJ:
                                xproj(fc, fd)
                            if k == SPLIT1:
                                dt_proj(fc, fd, 0)
                                split(fc, fd, 1)
                            if k == SPLIT2:
                                dt_proj(fc, fd, 1)
                                split(fc, fd, 2)
                        if tail and k == TAIL_AT:
                            out_proj(i - 1, 0)
                            out_proj(i - 1, 1)
                        if more and k == TURN:
                            turn(i + 1)
                        if front:
                            for n in c_beside(k, 1):
                                spread_c(fc, fd, n)
                        if before:
                            add_up(before)

            chunks(pe, chunk)
            for k in range(UNITS - LAG, UNITS):
                add_up((NCH - 1, 1, k))
            out_proj(NCH - 1, 0)
            out_proj(NCH - 1, 1)

        @block.scalar
        def _(act):
            act.wait_ge(loaded, LOADED)
            act.activation(a_neg[:], a_neg[:], ACT.Exp).then_inc(setup_act, 1)

            def bank(c, what, d=0, n=0):
                act.wait_ge(job_filled, job(c, what, d, n))
                return m_ps[bank_of(c, what, d, n)]

            def tokens(c):
                if late(c):
                    act.wait_ge(h0b_taken, c)
                m = bank(c, "tokens")
                act.activation(h0[:].rearrange("p j n -> p (j n)"), m[0:TP, :], ACT.Copy).then_inc(job_drained, 1)

            def norm_z(c):
                act.wait_ge(ln_ready[0], c + 1)
                if late(c):
                    act.wait_ge(z_taken, c)
                for j in range(NT):
                    op = act.activation(z[:, j, :], h0[:, j, :], ACT.Identity, bias=shift[:, 0, j:j + 1],
                                        scale=rstd[:, 0, j:j + 1])
                op.then_inc(z_ready, 1)

            def take_z(c):
                act.wait_ge(z_ready, c + 1)
                if late(c):
                    act.wait_ge(kept, c)
                act.activation(z_now[:], z[:], ACT.Copy).then_inc(z_taken, 1)

            def keep(c):
                act.wait_ge(h0b_taken, c + 1)
                act.wait_ge(z_taken, c + 1)
                if late(c):
                    act.wait_ge(h1_ready, c)
                act.activation(h0b_kept[:], h0b_now[:], ACT.Copy)
                act.activation(z_kept[:], z_now[:], ACT.Copy).then_inc(kept, 1)

            def turned(c):
                m = bank(c, "turn")
                act.activation(zt[:, :, PAD:PAD + T], m[:, 0:TC].rearrange("p (s t) -> p s t", s=SC),
                               ACT.Copy).then_inc(job_drained, 1)

            def silus(c, d):
                if late(4 * c + (2 * d - 2)):
                    act.wait_ge(y_read, 4 * c + (2 * d - 2))
                for db in range(2):
                    m = bank(c, "conv", d, db)
                    act.activation(xc[d][:, db, :], m[:, 0:TC], ACT.Silu,
                                   bias=convb[:, d, db:db + 1]).then_inc(job_drained, 1)

            def gates(c, d, db):
                if late(4 * c + (2 * d - 2)):
                    act.wait_ge(yg_ready, 4 * c + (2 * d - 2))
                m = bank(c, "gate", d, db)
                act.activation(gate[d][:, db, :], m[:, 0:TC], ACT.Silu).then_inc(job_drained, 1)

            def xproj(c, d):
                if late(nth(c, d, 0) - UNITS):
                    act.wait_ge(b_filled, nth(c, d, 0) - UNITS)
                m = bank(c, "xproj", d)
                act.activation(dbl[DT0:XR, :], m[DT0:XR, 0:TC], ACT.Copy)
                act.activation(parts[d][:], m[0:K2, 0:TC], ACT.Copy).then_inc(job_drained, 1)

            def split(c, d, n):
                m = bank(c, "split", d, n)
                act.activation(parts[d][:], m[0:K2, 0:TC], ACT.Copy).then_inc(job_drained, 1)

            def out_half(c, part):
                if late(c):
                    act.wait_ge(out_ready, c)
                m = bank(c, "tail", 0, part)
                act.activation(s[:, 2 * part:2 * part + 2, :].rearrange("p j n -> p (j n)"), m[0:TP, 0:2 * DM],
                               ACT.Copy, scale=0.5).then_inc(job_drained, 1)

            def dt_parts(c, d, db):
                if late(2 * c + d):
                    act.wait_ge(u_ready, 2 * c + d)
                m = bank(c, "dt", d, db)
                act.activation(e_neg[:, db, :], m[:, 0:TC], ACT.Abs, bias=dtb[:, d, db:db + 1])
                act.activation(relu[:, db, :], m[:, 0:TC], ACT.Relu,
                               bias=dtb[:, d, db:db + 1]).then_inc(job_drained, 1)

            def softplus(c, d):
                act.wait_ge(job_drained, job(c, "dt", d, 1))
                act.activation(e_neg[:], e_neg[:], ACT.Exp, scale=-1.0).then_inc(exp_ready, 1)
                act.wait_ge(exp_ready, 2 * c + (d + 1))
                act.activation(e_one[:], e_neg[:], ACT.Identity, bias=ones[:, 0:1])
                act.activation(log1[:], e_neg[:], ACT.Ln, bias=ones[:, 0:1]).then_inc(sp_ready, 1)

            def spread_c(c, d, n):
                if late(nth(c, d, 0) - UNITS + (PAIRS + n // 2 + 1)):
                    act.wait_ge(hc_ready, nth(c, d, 0) - UNITS + (PAIRS + n // 2 + 1))
                m = bank(c, "c", d, n)
                act.activation(c_all[:, n, :], m[:, 0:TC], ACT.Copy).then_inc(job_drained, 1)

            def norm_q(c):
                act.wait_ge(ln_ready[1], c + 1)
                for j in range(NT):
                    op = act.activation(s[:, j, :], s[:, j, :], ACT.Identity, bias=shift[:, 1, j:j + 1],
                                        scale=rstd[:, 1, j:j + 1])
                op.then_inc(q_ready, 1)

            def norm_out(c):
                if late(16 * c):
                    act.wait_ge(out_stored, 16 * c)
                act.wait_ge(ln_ready[2], c + 1)
                for j in range(NT):
                    op = act.activation(out_sb[:, j, :], s[:, j, :], ACT.Identity, bias=shift[:, 2, j:j + 1],
                                        scale=gain[:, j:j + 1])
                op.then_inc(out_ready, 1)

            def decay(unit):
                i, d, k = unit
                if k == 0:
                    act.wait_ge(delta_ready, 2 * i + (d + 1))
                if late(nth(*unit) - (RING - 1)):
                    act.wait_ge(scanned, nth(*unit) - (RING - 1))
                db, r = k // PAIRS, 2 * (k % PAIRS)
                steps = delta[d][:, db, :].rearrange("p (s t) -> p s t", s=SC)[:, :, 1:T]
                for j in range(2):
                    op = act.activation(da[k % RING][:, j, :, 1:T], steps, ACT.Exp,
                                        scale=a_neg[:, d, db, r + j:r + j + 1])
                op.then_inc(da_ready, 1)

            act.wait_ge(setup_dve, SETUP_DVE)
            tokens(0)
            norm_z(0)
            turned(0)
            silus(0, 0)
            gates(0, 0, 0)
            gates(0, 0, 1)
            xproj(0, 0)
            for db in range(2):
                dt_parts(0, 0, db)
                split(0, 0, db + 1)
            softplus(0, 0)
            take_z(0)
            for _, n in C_FIRST:
                spread_c(0, 0, n)
            for k in range(2):
                decay((0, 0, k))

            def chunk(i):
                for d in range(2):
                    fc, fd = (i, 1) if d == 0 else (i + 1, 0)
                    front, tail, more = beside(i, d)
                    for k in range(UNITS):
                        later = ahead(i, d, k, 2)
                        if later:
                            decay(later)
                        for n in c_beside(k, 0):
                            spread_c(i, d, n)
                        if more and k == TOKENS:
                            tokens(i + 1)
                        if front:
                            if k == SILU:
                                silus(fc, fd)
                                gates(fc, fd, 0)
                                gates(fc, fd, 1)
                            if k == XPROJ:
                                xproj(fc, fd)
                            if k == SPLIT1:
                                dt_parts(fc, fd, 0)
                                split(fc, fd, 1)
                            if k == SPLIT2:
                                dt_parts(fc, fd, 1)
                                split(fc, fd, 2)
                                softplus(fc, fd)
                        if more and k == NORM_Z:
                            norm_z(i + 1)
                        if tail and k == TAIL_AT:
                            out_half(i - 1, 0)
                            out_half(i - 1, 1)
                        if more and k == TURN:
                            turned(i + 1)
                        if front:
                            for n in c_beside(k, 1):
                                spread_c(fc, fd, n)
                        if tail and k == NORM_Q:
                            norm_q(i - 1)
                        if d == 1:
                            if k == KEEP:
                                keep(i)
                            if k == TAKE and not last(i):
                                take_z(i + 1)
                            if k == NORM_OUT and not (isinstance(i, int) and i == 0):
                                norm_out(i - 1)

            chunks(act, chunk)
            out_half(NCH - 1, 0)
            out_half(NCH - 1, 1)
            norm_q(NCH - 1)
            norm_out(NCH - 1)

        @block.gpsimd
        def _(pool):
            pool.memset(half[:], -0.5).then_inc(setup_pool, 1)
            pool.wait_ge(loaded, LOADED)

            def spread(row):
                return row[:].unsqueeze(1).broadcast_to([TP, NT, DM])

            def power(n, c):
                pool.wait_ge(ln_step[n], 3 * c + 3)
                pool.tensor_tensor(rstd[:, n, :], vareps[:, n, :], half[:], ALU.pow).then_inc(ln_pow[n], 1)

            def take_h0(c):
                if late(c):
                    pool.wait_ge(kept, c)
                pool.wait_ge(z_ready, c + 1)
                pool.tensor_tensor(h0b_now[:], h0[:], spread(lnb), ALU.add).then_inc(h0b_taken, 1)

            def softplus(c, d, piece):
                if piece == 0:
                    pool.wait_ge(lost_ready, 2 * c + (d + 1))
                    pool.tensor_tensor(log1[:], log1[:], e_one[:], ALU.subtract).then_inc(sp_step, 1)
                if piece == 1:
                    pool.wait_ge(sp_step, 2 * c + (d + 1))
                    if late(nth(c, d, 0) - UNITS):
                        pool.wait_ge(da_ready, nth(c, d, 0) - UNITS)
                    pool.tensor_tensor(delta[d][:], log1[:], relu[:], ALU.add).then_inc(delta_ready, 1)
                if piece == 2:
                    pool.wait_ge(delta_ready, 2 * c + (d + 1))
                    if late(nth(c, d, 0) - UNITS):
                        pool.wait_ge(dbx_ready, nth(c, d, 0) - UNITS)
                    pool.tensor_tensor(u[d][:], delta[d][:], xc[d][:], ALU.mult).then_inc(u_ready, 1)

            def times_c(unit):
                i, d, k = unit
                r = 2 * (k % PAIRS)
                if k < PAIRS:
                    pool.wait_ge(job_drained, job(i, "c", d, r + 1))
                pool.wait_ge(scanned, nth(*unit) + 1)
                pool.tensor_tensor(h[k % HRING][:], h[k % HRING][:],
                                   c_all[:, r:r + 2, :].rearrange("p n t -> p (n t)"), ALU.mult)\
                    .then_inc(hc_ready, 1)

            def gated(i, d, db):
                pool.wait_ge(y_read, 4 * i + (2 * d + db + 1))
                pool.wait_ge(job_drained, job(i, "gate", d, db))
                if not (isinstance(i, int) and i == 0):
                    pool.wait_ge(job_filled, job(i - 1, "tail", 0, 1))
                dst = yg[d][:, db, :].rearrange("p (s t) -> p s t", s=SC)
                dst = dst if d == 0 else dst[:, :, ::-1]
                pool.tensor_tensor(dst, yv[:, db, :].rearrange("p (s t) -> p s t", s=SC),
                                   gate[d][:, db, :].rearrange("p (s t) -> p s t", s=SC),
                                   ALU.mult).then_inc(yg_ready, 1)

            def add_z(c):
                pool.wait_ge(job_drained, job(c, "tail", 0, 1))
                pool.wait_ge(kept, c + 1)
                pool.tensor_tensor(s[:], s[:], z_kept[:], ALU.add).then_inc(s_ready, 1)

            def residual(c):
                pool.wait_ge(q_ready, c + 1)
                pool.tensor_tensor(s[:], s[:], spread(lng), ALU.mult).then_inc(h1_step, 1)
                pool.wait_ge(h1_step, c + 1)
                pool.tensor_tensor(s[:], s[:], h0b_kept[:], ALU.add).then_inc(h1_ready, 1)

            pool.wait_ge(setup_pool, 1)
            power(0, 0)
            take_h0(0)
            for piece in range(3):
                softplus(0, 0, piece)

            def chunk(i):
                for d in range(2):
                    fc, fd = (i, 1) if d == 0 else (i + 1, 0)
                    front, tail, more = beside(i, d)
                    for k in range(UNITS):
                        before = back(i, d, k, 1)
                        if before:
                            times_c(before)
                        if k == SKIP1 and back(i, d, k, UNITS):
                            gated(*back(i, d, k, UNITS)[:2], 1)
                        if k == SKIP0:
                            gated(i, d, 0)
                        if front and SOFTPLUS <= k < SOFTPLUS + 3:
                            softplus(fc, fd, k - SOFTPLUS)
                        if more and k == POW_Z:
                            power(0, i + 1)
                        if tail and k == ADD_Z:
                            add_z(i - 1)
                        if tail and k == POW_Q:
                            power(1, i - 1)
                        if d == 1:
                            if k == RESIDUAL and not (isinstance(i, int) and i == 0):
                                residual(i - 1)
                            if k == POW_OUT and not (isinstance(i, int) and i == 0):
                                power(2, i - 1)
                            if k == TAKE and not last(i):
                                take_h0(i + 1)

            chunks(pool, chunk)
            times_c((NCH - 1, 1, UNITS - 1))
            gated(NCH - 1, 1, 1)
            add_z(NCH - 1)
            power(1, NCH - 1)
            residual(NCH - 1)
            power(2, NCH - 1)

        @block.vector
        def _(dve):
            dve.memset(zt[:], 0.0).then_inc(setup_dve, 1)
            for j in range(RING):
                dve.memset(da[j][:], 0.0).then_inc(setup_dve, 1)
            dve.memset(xin[K2:K2 + 1, :, :], 1.0).then_inc(setup_dve, 1)
            dve.memset(ones[:], 1.0).then_inc(setup_dve, 1)
            dve.wait_ge(loaded, LOADED)
            dve.tensor_copy(pick[:], eyes[:].unsqueeze(2).broadcast_to([K2, 32, 128])).then_inc(setup_dve, 1)
            dve.tensor_copy(minus[:], minus32[:]).then_inc(setup_dve, 1)
            for d in range(2):
                for k in range(TAPS):
                    dve.tensor_tensor(convw[d][:, k, :], inw[d][:, 0:DI], cwb[:, d, k, :],
                                      ALU.mult).then_inc(setup_dve, 1)
            dve.wait_ge(setup_act, 1)
            dve.tensor_scalar(a_neg[:], a_neg[:], -1.0, None, ALU.mult).then_inc(setup_dve, 1)

            def statistics(n, src, c):
                for j in range(NT):
                    op = dve.bn_stats(stats[:, n, j, :], src[:, j, :])
                op.then_inc(ln_step[n], 1)
                dve.wait_ge(ln_step[n], 3 * c + 1)
                dve.memset(vareps[:, n, :], EPS)
                for j in range(NT):
                    op = dve.bn_aggr(meanvar[:, n, j, :], stats[:, n, j, :])
                op.then_inc(ln_step[n], 1)
                dve.wait_ge(ln_step[n], 3 * c + 2)
                dve.tensor_tensor(vareps[:, n, :], vareps[:, n, :], meanvar[:, n, :, 1],
                                  ALU.add).then_inc(ln_step[n], 1)

            def shifts(n, c):
                dve.wait_ge(ln_pow[n], c + 1)
                if n == 2:
                    dve.tensor_scalar(gain[:], rstd[:, n, :], 1.0, None, ALU.add)
                dve.scalar_tensor_tensor(out=shift[:, n, :], in0=meanvar[:, n, :, 0], scalar=-1.0,
                                         in1=rstd[:, n, :], op0=ALU.mult, op1=ALU.mult).then_inc(ln_ready[n], 1)

            def times_b(unit):
                i, d, k = unit
                if k == 0:
                    dve.wait_ge(u_ready, 2 * i + (d + 1))
                dve.wait_ge(b_filled, nth(*unit) + 1)
                g = g_ps[k % 2][:, 0:UC].rearrange("p (n t) -> p n t", n=2)
                dve.tensor_tensor(g, u[d][:, k // PAIRS, :].unsqueeze(1).broadcast_to([128, 2, TC]), g,
                                  ALU.mult).then_inc(dbx_ready, 1)

            def scan(unit):
                i, d, k = unit
                n = nth(*unit)
                dve.wait_ge(da_ready, n + 1)
                if late(n - (HRING - 1)):
                    dve.wait_ge(summed, n - (HRING - 1))
                dve.wait_ge(dbx_ready, n + 1)
                dve.tensor_tensor_scan(h[k % HRING][:], da[k % RING][:].rearrange("p n s t -> p (n s t)"),
                                       g_ps[k % 2][:, 0:UC], 0.0, ALU.mult, ALU.add).then_inc(scanned, 1)

            def skip(i, d, db):
                at = 4 * i + (2 * d + db)
                dve.wait_ge(summed, nth(i, d, PAIRS * (db + 1)))
                if late(at - 1):
                    dve.wait_ge(yg_ready, at - 1)
                dve.scalar_tensor_tensor(out=yv[:, db, :], in0=xc[d][:, db, :], scalar=dskip[:, d, db:db + 1],
                                         in1=y_ps[db][:, 0:TC], op0=ALU.mult, op1=ALU.add).then_inc(y_read, 1)

            def log_terms(c, d):
                dve.wait_ge(sp_ready, 2 * c + (d + 1))
                dve.scalar_tensor_tensor(out=log1[:], in0=e_one[:], scalar=1.0, in1=log1[:],
                                         op0=ALU.is_gt, op1=ALU.mult).then_inc(masked, 1)
                dve.wait_ge(masked, 2 * c + (d + 1))
                dve.scalar_tensor_tensor(out=e_one[:], in0=e_one[:], scalar=-1.0, in1=e_neg[:],
                                         op0=ALU.add, op1=ALU.subtract).then_inc(lost_ready, 1)

            dve.wait_ge(job_drained, job(0, "tokens"))
            statistics(0, h0, 0)
            shifts(0, 0)
            log_terms(0, 0)

            def chunk(i):
                for d in range(2):
                    fc, fd = (i, 1) if d == 0 else (i + 1, 0)
                    front, tail, more = beside(i, d)
                    for k in range(UNITS):
                        if k == SKIP1 and back(i, d, k, UNITS):
                            skip(*back(i, d, k, UNITS)[:2], 1)
                        if k == SKIP0:
                            skip(i, d, 0)
                        times_b((i, d, k))
                        scan((i, d, k))
                        if more and k == STATS_Z:
                            dve.wait_ge(job_drained, job(i + 1, "tokens"))
                            dve.wait_ge(z_ready, i + 1)
                            statistics(0, h0, i + 1)
                        if more and k == SHIFT_Z:
                            shifts(0, i + 1)
                        if front and k == LOG:
                            log_terms(fc, fd)
                        if tail and k == STATS_Q:
                            dve.wait_ge(s_ready, i)
                            if late(i - 1):
                                dve.wait_ge(q_ready, i - 1)
                            statistics(1, s, i - 1)
                        if tail and k == SHIFT_Q:
                            shifts(1, i - 1)
                        if d == 1 and not (isinstance(i, int) and i == 0):
                            if k == STATS_OUT:
                                dve.wait_ge(h1_ready, i)
                                if late(i - 1):
                                    dve.wait_ge(out_ready, i - 1)
                                statistics(2, s, i - 1)
                            if k == SHIFT_OUT:
                                shifts(2, i - 1)

            chunks(dve, chunk)
            skip(NCH - 1, 1, 1)
            for n, ready in ((1, s_ready), (2, h1_ready)):
                dve.wait_ge(ready, NCH)
                dve.wait_ge((q_ready, out_ready)[n - 1], NCH - 1)
                statistics(n, s, NCH - 1)
                shifts(n, NCH - 1)


def kernel(x, L0_tok_weight, L0_tok_bias, L0_attn_ln_g, L0_attn_ln_b, L0_ffn_W, L0_ffn_b, **attn):
    import numpy as np
    import concourse.bacc as bacc
    from concourse.bass_utils import run_bass_kernel_spmd

    nc = bacc.Bacc("TRN2", target_bir_lowering=False, num_devices=1)
    arrays = {}

    def given(name, a):
        arrays[name] = np.ascontiguousarray(a)
        return nc.dram_tensor(name, arrays[name].shape, mybir.dt.from_np(arrays[name].dtype), kind="ExternalInput").ap()

    def halves(a):
        return np.moveaxis(np.asarray(a).reshape(2, 128, *np.asarray(a).shape[1:]), 0, 1)

    tokens = np.asarray(x).reshape(SEQS * T, 2 * K2)
    x_t = given("x_t", tokens.T.reshape(2, K2, SEQS * T))
    tok_w = given("tok_w", np.asarray(L0_tok_weight).T.reshape(2, K2, DM))
    tok_b = given("tok_b", np.asarray(L0_tok_bias).reshape(1, DM))
    dirs = []
    for d in "fb":
        w = {k[len("L0_attn_f_"):]: np.asarray(v) for k, v in attn.items() if k.startswith(f"L0_attn_{d}_")}
        dt_rows, bc_rows = w["x_proj"][:RANK], w["x_proj"][RANK:]
        rows = np.concatenate([bc_rows, bc_rows, bc_rows, dt_rows])
        dirs.append((given(f"{d}_in_w", w["in_proj"].T), given(f"{d}_conv_w", w["conv_w"].T),
                     given(f"{d}_conv_b", halves(w["conv_b"])), given(f"{d}_xproj_w", halves(rows.T)),
                     given(f"{d}_dt_w", w["dt_w"].T), given(f"{d}_dt_b", halves(w["dt_b"])),
                     given(f"{d}_a_log", halves(w["A_log"])), given(f"{d}_d_skip", halves(w["Dv"])),
                     given(f"{d}_out_w", halves(w["out_proj"].T))))
    ln_g, ln_b = given("ln_g", L0_attn_ln_g), given("ln_b", L0_attn_ln_b)
    eye = given("eye", np.eye(128, dtype=np.float32))
    eye3 = given("eye3", np.tile(np.eye(32, dtype=np.float32), (3, 1)))
    minus = np.zeros((K2, 2, K2), np.float32)
    for n in range(2):
        for row in range(32 * (n + 1), K2):
            minus[row, n, row] = -1.0
    minus_eye = given("minus_eye", minus)
    out = nc.dram_tensor("out", (SEQS * T, DM), F32, kind="ExternalOutput").ap()
    audio_tower_kernel(nc, x_t, tok_w, tok_b, dirs, ln_g, ln_b, eye, eye3, minus_eye, out)
    r = run_bass_kernel_spmd(nc, [arrays], core_ids=[0])
    return r.results[0]["out"].reshape(SEQS, T, DM)
```
